# Optimizing a Trainium2 kernel written in Bass

```python
import numpy as np
import jax
import jax.numpy as jnp

def _softmax(x, axis=-1):
    return jax.nn.softmax(x, axis=axis)

def _gelu(x):
    return jax.nn.gelu(x, approximate=True)

def _silu(x):
    return jax.nn.silu(x)

def _sigmoid(x):
    return jax.nn.sigmoid(x)

def _layernorm(x, axis=-1, eps=1e-05):
    m = jnp.mean(x, axis=axis, keepdims=True)
    v = jnp.var(x, axis=axis, keepdims=True)
    return (x - m) / jnp.sqrt(v + eps)

def _scatter_add(tgt, idx, src, axis=0):
    return tgt.at[idx].add(src)

def _segment_sum(src, seg, n):
    return jax.ops.segment_sum(src, seg, n)
kernel_name = 'mk_decoder_postln_d2_seqx_r4_19e76b'

def setup_inputs(seed: int=0):
    np.random.seed(seed)
    _w = jnp.asarray

    def _rec_inputs():
        import jax
        import jax.numpy as jnp
        _rk = jax.random.key(seed)
        x = -0.000125 + 0.9999 * jax.random.normal(jax.random.fold_in(_rk, 1), (4, 512, 512), jnp.float32)
        _lenS = 512 - jax.random.randint(jax.random.fold_in(_rk, 7), (4,), 0, max(1, 512 // 4) + 1, jnp.int32)
        _lenS2 = 512 - jax.random.randint(jax.random.fold_in(_rk, 8), (4,), 0, max(1, 512 // 4) + 1, jnp.int32)
        fside_BxS2xS2_0 = -3.05549e-07 + 0.0199987 * jax.random.normal(jax.random.fold_in(_rk, 11), (4, 512, 512), jnp.float32)
        _ctx_1024P = jax.random.normal(jax.random.fold_in(_rk, 12), (4, 16, 256), jnp.float32)
        _ctx_1024c = jax.random.dirichlet(jax.random.fold_in(_rk, 512), 0.3 * jnp.ones((16,), jnp.float32), (4, 512))
        _ctx_1024t = jnp.einsum('bsk,bkd->bsd', _ctx_1024c, _ctx_1024P)
        _ctx_1024t = _ctx_1024t * jax.lax.rsqrt(jnp.mean(jnp.square(_ctx_1024t)) + 1e-12) * 0.953939
        ctx_1024 = 6.82029e-06 + 0.0200006 * (_ctx_1024t + 0.3 * jax.random.normal(jax.random.fold_in(_rk, 612), (4, 512, 256), jnp.float32))
        return (x, fside_BxS2xS2_0, ctx_1024)
    x, fside_BxS2xS2_0, ctx_1024 = _rec_inputs()

    def _L0_attn_setup():
        import jax, jax.numpy as jnp
        import numpy as np
        B_, L_, H_, D_, N_, TR_, K_ = (2, 512, 512, 1024, 16, 128, 4)

        def _silu(x):
            return x * jax.nn.sigmoid(x)

        def _causal_dwconv(x, w, b):
            k = w.shape[-1]
            out = jax.lax.conv_general_dilated(x, w[:, None, :], window_strides=(1,), padding=[(k - 1, 0)], dimension_numbers=('NCH', 'OIH', 'NCH'), feature_group_count=x.shape[1])
            return out + b[None, :, None]
        key = jax.random.key(seed)
        ks = jax.random.split(key, 9)
        g = lambda k, shape, s: jax.random.normal(k, shape, dtype=jnp.float32) * s
        A = jnp.broadcast_to(jnp.arange(1, N_ + 1, dtype=jnp.float32)[None, :], (D_, N_))
        return {'hidden_states': g(ks[0], (B_, L_, H_), 1.0), 'in_proj_w': g(ks[1], (2 * D_, H_), 0.02), 'conv_w': g(ks[2], (D_, K_), 0.5), 'conv_b': g(ks[3], (D_,), 0.1), 'x_proj_w': g(ks[4], (TR_ + 2 * N_, D_), 0.02), 'dt_proj_w': g(ks[5], (D_, TR_), 0.02), 'dt_proj_b': g(ks[6], (D_,), 0.1), 'A_log': jnp.log(A), 'D': jnp.ones((D_,), jnp.float32), 'out_proj_w': g(ks[7], (H_, D_), 0.02)}
    _L0_attn_all = _L0_attn_setup()
    _L0_attn_in = {k: v for k, v in _L0_attn_all.items() if k in ('in_proj_w', 'conv_w', 'conv_b', 'x_proj_w', 'dt_proj_w', 'dt_proj_b', 'A_log', 'D', 'out_proj_w')}
    del _L0_attn_all

    def _L0_xattn_setup():
        import jax, jax.numpy as jnp
        import numpy as np
        EPS = 1e-06
        QMAX = 127.0

        def _smooth_quant_linear(x, w):
            amax_x = jnp.max(jnp.abs(x), axis=0)
            amax_w = jnp.max(jnp.abs(w), axis=0)
            s = jnp.sqrt(jnp.maximum(amax_x, EPS) / jnp.maximum(amax_w, EPS))
            s = jnp.maximum(s, EPS)
            xs = x / s
            ws = w * s
            x_scale = jnp.maximum(jnp.max(jnp.abs(xs), axis=-1, keepdims=True), EPS) / QMAX
            w_scale = jnp.maximum(jnp.max(jnp.abs(ws), axis=-1, keepdims=True), EPS) / QMAX
            x_q = jnp.clip(jnp.round(xs / x_scale), -QMAX, QMAX)
            w_q = jnp.clip(jnp.round(ws / w_scale), -QMAX, QMAX)
            return x_q @ w_q.T * x_scale * w_scale.T

        def _expert_forward(xe, guw, dw):
            h = _smooth_quant_linear(xe, guw)
            gate, up = jnp.split(h, 2, axis=-1)
            a = jax.nn.silu(gate) * up
            return _smooth_quant_linear(a, dw)
        key = jax.random.key(seed)
        k1, k2, k3 = jax.random.split(key, 3)
        E, T, D, I = (8, 512, 512, 256)
        x = jax.random.normal(k1, (E, T, D), dtype=jnp.float32)
        gate_up_weight = jax.random.normal(k2, (E, 2 * I, D), dtype=jnp.float32) * 0.02
        down_weight = jax.random.normal(k3, (E, D, I), dtype=jnp.float32) * 0.02
        return {'x': x, 'gate_up_weight': gate_up_weight, 'down_weight': down_weight}
    _L0_xattn_all = _L0_xattn_setup()
    _L0_xattn_in = {k: v for k, v in _L0_xattn_all.items() if k in ()}
    del _L0_xattn_all

    def _L0_ffn_setup():
        import jax, jax.numpy as jnp
        import numpy as np
        DIM_IN = 512
        DIM_HIDDEN = 2048
        key = jax.random.key(seed)
        k_x, k_g, k_u, k_d = jax.random.split(key, 4)
        s_in = 1.0 / np.sqrt(DIM_IN)
        s_hid = 1.0 / np.sqrt(DIM_HIDDEN)
        x = jax.random.normal(k_x, (4, 512, DIM_IN), dtype=jnp.float32)
        w_gate = jax.random.uniform(k_g, (DIM_HIDDEN, DIM_IN), jnp.float32, -s_in, s_in)
        w_up = jax.random.uniform(k_u, (DIM_HIDDEN, DIM_IN), jnp.float32, -s_in, s_in)
        w_down = jax.random.uniform(k_d, (DIM_IN, DIM_HIDDEN), jnp.float32, -s_hid, s_hid)
        return {'x': x, 'w_gate': w_gate, 'w_up': w_up, 'w_down': w_down}
    _L0_ffn_all = _L0_ffn_setup()
    _L0_ffn_in = {k: v for k, v in _L0_ffn_all.items() if k in ('w_gate', 'w_up', 'w_down')}
    del _L0_ffn_all

    def _L1_attn_setup():
        import jax, jax.numpy as jnp
        import numpy as np
        HID = 512
        NH = 32
        DK = 256
        DV = 512
        HQK = DK // NH
        HV = DV // NH
        RLO = 32
        GLO = 64
        EPS = 1e-05
        B, L = (4, 1024)

        def _forward(x, mu_x, Wx1, Wx2, Wr, Ww1, Ww2, bw, Wk, Wv, Wg, bonus, gn_w, gn_b, Wo):
            Bn, Ln, _ = x.shape
            delta = jnp.pad(x[:, :-1], ((0, 0), (1, 0), (0, 0))) - x
            z = jnp.tanh((x + delta * mu_x) @ Wx1).reshape(Bn, Ln, 5, RLO)
            mus = jnp.einsum('blnr,nrd->blnd', z, Wx2)
            mr, mw, mk, mv, mg = (mus[:, :, i] for i in range(5))
            r = (x + delta * mr) @ Wr
            w = jnp.tanh((x + delta * mw) @ Ww1) @ Ww2 + bw
            k = (x + delta * mk) @ Wk
            v = (x + delta * mv) @ Wv
            g = (x + delta * mg) @ Wg
            heads = lambda t, d: t.reshape(Bn, Ln, NH, d).transpose(1, 0, 2, 3)
            r_t, k_t = (heads(r, HQK), heads(k, HQK))
            v_t = heads(v, HV)
            decay = jnp.exp(-jnp.exp(heads(w, HQK)))

            def step(S, inp):
                rt, kt, vt, dt = inp
                kv = kt[..., :, None] * vt[..., None, :]
                ot = jnp.einsum('bhk,bhkv->bhv', rt, S + bonus[None, :, :, None] * kv)
                return (S * dt[..., :, None] + kv, ot)
            S0 = jnp.zeros((Bn, NH, HQK, HV), x.dtype)
            _, o = jax.lax.scan(step, S0, (r_t, k_t, v_t, decay))
            o = o.transpose(1, 0, 2, 3)
            mean = o.mean(-1, keepdims=True)
            var = o.var(-1, keepdims=True)
            on = (o - mean) * jax.lax.rsqrt(var + EPS) * gn_w + gn_b
            gh = g.reshape(Bn, Ln, NH, HV)
            o = on * (gh * jax.nn.sigmoid(gh))
            return o.reshape(Bn, Ln, DV) @ Wo
        key = jax.random.key(seed)
        ks = jax.random.split(key, 16)
        s = 0.02
        return {'hidden_states': jax.random.normal(ks[0], (B, L, HID), jnp.float32), 'mu_x': jax.random.uniform(ks[1], (HID,), jnp.float32), 'Wx1': jax.random.normal(ks[2], (HID, 5 * RLO), jnp.float32) * s, 'Wx2': jax.random.normal(ks[3], (5, RLO, HID), jnp.float32) * s, 'Wr': jax.random.normal(ks[4], (HID, DK), jnp.float32) * s, 'Ww1': jax.random.normal(ks[5], (HID, GLO), jnp.float32) * s, 'Ww2': jax.random.normal(ks[6], (GLO, DK), jnp.float32) * s, 'bw': jnp.zeros((DK,), jnp.float32), 'Wk': jax.random.normal(ks[7], (HID, DK), jnp.float32) * s, 'Wv': jax.random.normal(ks[8], (HID, DV), jnp.float32) * s, 'Wg': jax.random.normal(ks[9], (HID, DV), jnp.float32) * s, 'bonus': jax.random.normal(ks[10], (NH, HQK), jnp.float32) * s, 'gn_w': jnp.ones((HV,), jnp.float32), 'gn_b': jnp.zeros((HV,), jnp.float32), 'Wo': jax.random.normal(ks[11], (DV, HID), jnp.float32) * s}
    _L1_attn_all = _L1_attn_setup()
    _L1_attn_in = {k: v for k, v in _L1_attn_all.items() if k in ('mu_x', 'Wx1', 'Wx2', 'Wr', 'Ww1', 'Ww2', 'bw', 'Wk', 'Wv', 'Wg', 'bonus', 'gn_w', 'gn_b', 'Wo')}
    del _L1_attn_all

    def _L1_xattn_setup():
        import jax, jax.numpy as jnp
        import numpy as np
        B_, L_, D_MODEL = (4, 512, 256)
        D_STATE, D_CONV, EXPAND = (16, 4, 2)
        D_INNER = EXPAND * D_MODEL
        DT_RANK = (D_MODEL + 15) // 16

        def silu(x):
            return x * jax.nn.sigmoid(x)
        key = jax.random.key(seed)
        ks = jax.random.split(key, 10)
        f32 = jnp.float32
        hidden_states = jax.random.normal(ks[0], (B_, L_, D_MODEL), dtype=f32)
        z = jax.random.normal(ks[1], (B_, D_INNER, L_), dtype=f32)
        in_proj_w = jax.random.normal(ks[2], (D_INNER, D_MODEL), dtype=f32) * 0.02
        conv_w = jax.random.normal(ks[3], (D_INNER, 1, D_CONV), dtype=f32) * 0.1
        conv_b = jax.random.normal(ks[4], (D_INNER,), dtype=f32) * 0.02
        x_proj_w = jax.random.normal(ks[5], (DT_RANK + 2 * D_STATE, D_INNER), dtype=f32) * 0.02
        dt_proj_w = jax.random.uniform(ks[6], (D_INNER, DT_RANK), dtype=f32, minval=-DT_RANK ** (-0.5), maxval=DT_RANK ** (-0.5))
        dt = jnp.exp(jax.random.uniform(ks[7], (D_INNER,), dtype=f32, minval=np.log(0.001), maxval=np.log(0.1)))
        dt_proj_b = jnp.log(jnp.expm1(dt))
        A_log = jnp.log(jnp.broadcast_to(jnp.arange(1, D_STATE + 1, dtype=f32), (D_INNER, D_STATE)))
        D = jnp.ones((D_INNER,), f32)
        return {'hidden_states': hidden_states, 'z': z, 'in_proj_w': in_proj_w, 'conv_w': conv_w, 'conv_b': conv_b, 'x_proj_w': x_proj_w, 'dt_proj_w': dt_proj_w, 'dt_proj_b': dt_proj_b, 'A_log': A_log, 'D': D}
    _L1_xattn_all = _L1_xattn_setup()
    _L1_xattn_in = {k: v for k, v in _L1_xattn_all.items() if k in ('in_proj_w', 'conv_w', 'conv_b', 'x_proj_w', 'dt_proj_w', 'dt_proj_b', 'A_log', 'D')}
    del _L1_xattn_all

    def _L1_ffn_setup():
        import jax, jax.numpy as jnp
        import numpy as np
        B, S, H = (2, 256, 512)
        E, K = (8, 2)
        F = 352
        FS = 1408
        NORM_TOPK = False

        def _swiglu(x, wg, wu, wd):
            return jax.nn.silu(x @ wg) * (x @ wu) @ wd
        key = jax.random.key(seed)
        ks = jax.random.split(key, 9)
        s = 0.02
        return {'hidden_states': jax.random.normal(ks[0], (B, S, H), dtype=jnp.float32), 'Wr': jax.random.normal(ks[1], (H, E), dtype=jnp.float32) * s, 'Wg': jax.random.normal(ks[2], (E, H, F), dtype=jnp.float32) * s, 'Wu': jax.random.normal(ks[3], (E, H, F), dtype=jnp.float32) * s, 'Wd': jax.random.normal(ks[4], (E, F, H), dtype=jnp.float32) * s, 'Sg': jax.random.normal(ks[5], (H, FS), dtype=jnp.float32) * s, 'Su': jax.random.normal(ks[6], (H, FS), dtype=jnp.float32) * s, 'Sd': jax.random.normal(ks[7], (FS, H), dtype=jnp.float32) * s, 'Wsg': jax.random.normal(ks[8], (H, 1), dtype=jnp.float32) * s}
    _L1_ffn_all = _L1_ffn_setup()
    _L1_ffn_in = {k: v for k, v in _L1_ffn_all.items() if k in ('Wr', 'Wg', 'Wu', 'Wd', 'Sg', 'Su', 'Sd', 'Wsg')}
    del _L1_ffn_all
    return {'x': x, 'fside_BxS2xS2_0': fside_BxS2xS2_0, 'ctx_1024': ctx_1024, 'L0_attn_in_proj_w': _L0_attn_in['in_proj_w'], 'L0_attn_conv_w': _L0_attn_in['conv_w'], 'L0_attn_conv_b': _L0_attn_in['conv_b'], 'L0_attn_x_proj_w': _L0_attn_in['x_proj_w'], 'L0_attn_dt_proj_w': _L0_attn_in['dt_proj_w'], 'L0_attn_dt_proj_b': _L0_attn_in['dt_proj_b'], 'L0_attn_A_log': _L0_attn_in['A_log'], 'L0_attn_D': _L0_attn_in['D'], 'L0_attn_out_proj_w': _L0_attn_in['out_proj_w'], 'L0_ffn_w_gate': _L0_ffn_in['w_gate'], 'L0_ffn_w_up': _L0_ffn_in['w_up'], 'L0_ffn_w_down': _L0_ffn_in['w_down'], 'L1_attn_mu_x': _L1_attn_in['mu_x'], 'L1_attn_Wx1': _L1_attn_in['Wx1'], 'L1_attn_Wx2': _L1_attn_in['Wx2'], 'L1_attn_Wr': _L1_attn_in['Wr'], 'L1_attn_Ww1': _L1_attn_in['Ww1'], 'L1_attn_Ww2': _L1_attn_in['Ww2'], 'L1_attn_bw': _L1_attn_in['bw'], 'L1_attn_Wk': _L1_attn_in['Wk'], 'L1_attn_Wv': _L1_attn_in['Wv'], 'L1_attn_Wg': _L1_attn_in['Wg'], 'L1_attn_bonus': _L1_attn_in['bonus'], 'L1_attn_gn_w': _L1_attn_in['gn_w'], 'L1_attn_gn_b': _L1_attn_in['gn_b'], 'L1_attn_Wo': _L1_attn_in['Wo'], 'L1_xattn_in_proj_w': _L1_xattn_in['in_proj_w'], 'L1_xattn_conv_w': _L1_xattn_in['conv_w'], 'L1_xattn_conv_b': _L1_xattn_in['conv_b'], 'L1_xattn_x_proj_w': _L1_xattn_in['x_proj_w'], 'L1_xattn_dt_proj_w': _L1_xattn_in['dt_proj_w'], 'L1_xattn_dt_proj_b': _L1_xattn_in['dt_proj_b'], 'L1_xattn_A_log': _L1_xattn_in['A_log'], 'L1_xattn_D': _L1_xattn_in['D'], 'L1_ffn_Wr': _L1_ffn_in['Wr'], 'L1_ffn_Wg': _L1_ffn_in['Wg'], 'L1_ffn_Wu': _L1_ffn_in['Wu'], 'L1_ffn_Wd': _L1_ffn_in['Wd'], 'L1_ffn_Sg': _L1_ffn_in['Sg'], 'L1_ffn_Su': _L1_ffn_in['Su'], 'L1_ffn_Sd': _L1_ffn_in['Sd'], 'L1_ffn_Wsg': _L1_ffn_in['Wsg']}

def reference(x, fside_BxS2xS2_0, ctx_1024, L0_attn_in_proj_w, L0_attn_conv_w, L0_attn_conv_b, L0_attn_x_proj_w, L0_attn_dt_proj_w, L0_attn_dt_proj_b, L0_attn_A_log, L0_attn_D, L0_attn_out_proj_w, L0_ffn_w_gate, L0_ffn_w_up, L0_ffn_w_down, L1_attn_mu_x, L1_attn_Wx1, L1_attn_Wx2, L1_attn_Wr, L1_attn_Ww1, L1_attn_Ww2, L1_attn_bw, L1_attn_Wk, L1_attn_Wv, L1_attn_Wg, L1_attn_bonus, L1_attn_gn_w, L1_attn_gn_b, L1_attn_Wo, L1_xattn_in_proj_w, L1_xattn_conv_w, L1_xattn_conv_b, L1_xattn_x_proj_w, L1_xattn_dt_proj_w, L1_xattn_dt_proj_b, L1_xattn_A_log, L1_xattn_D, L1_ffn_Wr, L1_ffn_Wg, L1_ffn_Wu, L1_ffn_Wd, L1_ffn_Sg, L1_ffn_Su, L1_ffn_Sd, L1_ffn_Wsg):
    import jax
    import jax.numpy as jnp

    def _L0_attn_ref(hidden_states, in_proj_w, conv_w, conv_b, x_proj_w, dt_proj_w, dt_proj_b, A_log, D, out_proj_w):
        import jax, jax.numpy as jnp
        import numpy as np
        B_, L_, H_, D_, N_, TR_, K_ = (2, 512, 512, 1024, 16, 128, 4)

        def _silu(x):
            return x * jax.nn.sigmoid(x)

        def _causal_dwconv(x, w, b):
            k = w.shape[-1]
            out = jax.lax.conv_general_dilated(x, w[:, None, :], window_strides=(1,), padding=[(k - 1, 0)], dimension_numbers=('NCH', 'OIH', 'NCH'), feature_group_count=x.shape[1])
            return out + b[None, :, None]
        d_inner = A_log.shape[0]
        n_state = A_log.shape[1]
        tr = dt_proj_w.shape[1]
        proj = jnp.einsum('blh,eh->ble', hidden_states, in_proj_w)
        hs, gate = (proj[..., :d_inner], proj[..., d_inner:])
        x_bdl = _silu(_causal_dwconv(hs.transpose(0, 2, 1), conv_w, conv_b))
        x = x_bdl.transpose(0, 2, 1)
        ssm = jnp.einsum('bld,pd->blp', x, x_proj_w)
        ts = ssm[..., :tr]
        Bm = ssm[..., tr:tr + n_state]
        Cm = ssm[..., tr + n_state:]
        dt = jax.nn.softplus(jnp.einsum('blr,dr->bld', ts, dt_proj_w) + dt_proj_b)
        A = -jnp.exp(A_log)

        def step(h, inp):
            dt_t, B_t, C_t, x_t = inp
            dA = jnp.exp(dt_t[:, :, None] * A[None])
            h = dA * h + (dt_t * x_t)[:, :, None] * B_t[:, None, :]
            y = jnp.einsum('bdn,bn->bd', h, C_t)
            return (h, y)
        xs = (dt.transpose(1, 0, 2), Bm.transpose(1, 0, 2), Cm.transpose(1, 0, 2), x.transpose(1, 0, 2))
        h0 = jnp.zeros((x.shape[0], d_inner, n_state), dtype=x.dtype)
        _, ys = jax.lax.scan(step, h0, xs)
        y = ys.transpose(1, 0, 2) + x * D[None, None, :]
        y = y * _silu(gate)
        return jnp.einsum('bld,hd->blh', y, out_proj_w)

    def _L0_xattn_ref(x, gate_up_weight, down_weight):
        import jax, jax.numpy as jnp
        import numpy as np
        EPS = 1e-06
        QMAX = 127.0

        def _smooth_quant_linear(x, w):
            amax_x = jnp.max(jnp.abs(x), axis=0)
            amax_w = jnp.max(jnp.abs(w), axis=0)
            s = jnp.sqrt(jnp.maximum(amax_x, EPS) / jnp.maximum(amax_w, EPS))
            s = jnp.maximum(s, EPS)
            xs = x / s
            ws = w * s
            x_scale = jnp.maximum(jnp.max(jnp.abs(xs), axis=-1, keepdims=True), EPS) / QMAX
            w_scale = jnp.maximum(jnp.max(jnp.abs(ws), axis=-1, keepdims=True), EPS) / QMAX
            x_q = jnp.clip(jnp.round(xs / x_scale), -QMAX, QMAX)
            w_q = jnp.clip(jnp.round(ws / w_scale), -QMAX, QMAX)
            return x_q @ w_q.T * x_scale * w_scale.T

        def _expert_forward(xe, guw, dw):
            h = _smooth_quant_linear(xe, guw)
            gate, up = jnp.split(h, 2, axis=-1)
            a = jax.nn.silu(gate) * up
            return _smooth_quant_linear(a, dw)
        return jax.vmap(_expert_forward)(x, gate_up_weight, down_weight)

    def _L0_ffn_ref(x, w_gate, w_up, w_down):
        import jax, jax.numpy as jnp
        import numpy as np
        DIM_IN = 512
        DIM_HIDDEN = 2048
        gate = jnp.einsum('bsd,hd->bsh', x, w_gate)
        up = jnp.einsum('bsd,hd->bsh', x, w_up)
        gated = jax.nn.silu(gate) * up
        return jnp.einsum('bsh,dh->bsd', gated, w_down)

    def _L1_attn_ref(hidden_states, mu_x, Wx1, Wx2, Wr, Ww1, Ww2, bw, Wk, Wv, Wg, bonus, gn_w, gn_b, Wo):
        import jax, jax.numpy as jnp
        import numpy as np
        HID = 512
        NH = 32
        DK = 256
        DV = 512
        HQK = DK // NH
        HV = DV // NH
        RLO = 32
        GLO = 64
        EPS = 1e-05
        B, L = (4, 1024)

        def _forward(x, mu_x, Wx1, Wx2, Wr, Ww1, Ww2, bw, Wk, Wv, Wg, bonus, gn_w, gn_b, Wo):
            Bn, Ln, _ = x.shape
            delta = jnp.pad(x[:, :-1], ((0, 0), (1, 0), (0, 0))) - x
            z = jnp.tanh((x + delta * mu_x) @ Wx1).reshape(Bn, Ln, 5, RLO)
            mus = jnp.einsum('blnr,nrd->blnd', z, Wx2)
            mr, mw, mk, mv, mg = (mus[:, :, i] for i in range(5))
            r = (x + delta * mr) @ Wr
            w = jnp.tanh((x + delta * mw) @ Ww1) @ Ww2 + bw
            k = (x + delta * mk) @ Wk
            v = (x + delta * mv) @ Wv
            g = (x + delta * mg) @ Wg
            heads = lambda t, d: t.reshape(Bn, Ln, NH, d).transpose(1, 0, 2, 3)
            r_t, k_t = (heads(r, HQK), heads(k, HQK))
            v_t = heads(v, HV)
            decay = jnp.exp(-jnp.exp(heads(w, HQK)))

            def step(S, inp):
                rt, kt, vt, dt = inp
                kv = kt[..., :, None] * vt[..., None, :]
                ot = jnp.einsum('bhk,bhkv->bhv', rt, S + bonus[None, :, :, None] * kv)
                return (S * dt[..., :, None] + kv, ot)
            S0 = jnp.zeros((Bn, NH, HQK, HV), x.dtype)
            _, o = jax.lax.scan(step, S0, (r_t, k_t, v_t, decay))
            o = o.transpose(1, 0, 2, 3)
            mean = o.mean(-1, keepdims=True)
            var = o.var(-1, keepdims=True)
            on = (o - mean) * jax.lax.rsqrt(var + EPS) * gn_w + gn_b
            gh = g.reshape(Bn, Ln, NH, HV)
            o = on * (gh * jax.nn.sigmoid(gh))
            return o.reshape(Bn, Ln, DV) @ Wo
        return _forward(hidden_states, mu_x, Wx1, Wx2, Wr, Ww1, Ww2, bw, Wk, Wv, Wg, bonus, gn_w, gn_b, Wo)

    def _L1_xattn_ref(hidden_states, z, in_proj_w, conv_w, conv_b, x_proj_w, dt_proj_w, dt_proj_b, A_log, D):
        import jax, jax.numpy as jnp
        import numpy as np
        B_, L_, D_MODEL = (4, 512, 256)
        D_STATE, D_CONV, EXPAND = (16, 4, 2)
        D_INNER = EXPAND * D_MODEL
        DT_RANK = (D_MODEL + 15) // 16

        def silu(x):
            return x * jax.nn.sigmoid(x)
        Bsz, L, _ = hidden_states.shape
        d_inner, _, d_conv = conv_w.shape
        dt_rank = dt_proj_w.shape[1]
        d_state = A_log.shape[1]
        x = jnp.einsum('bld,ed->bel', hidden_states, in_proj_w)
        xc = jax.lax.conv_general_dilated(x, conv_w, window_strides=(1,), padding=[(d_conv - 1, 0)], feature_group_count=d_inner, dimension_numbers=('NCH', 'OIH', 'NCH'))
        x = silu(xc + conv_b[None, :, None])
        x_dbl = jnp.einsum('bdl,ed->bel', x, x_proj_w)
        dt_low, Bm, Cm = jnp.split(x_dbl, [dt_rank, dt_rank + d_state], axis=1)
        dt = jnp.einsum('brl,dr->bdl', dt_low, dt_proj_w)
        dt = jax.nn.softplus(dt + dt_proj_b[None, :, None])
        A = -jnp.exp(A_log)
        dt_t = jnp.moveaxis(dt, -1, 0)
        B_t = jnp.moveaxis(Bm, -1, 0)
        C_t = jnp.moveaxis(Cm, -1, 0)
        u_t = jnp.moveaxis(x, -1, 0)

        def step(state, inp):
            d, b, c, u = inp
            dA = jnp.exp(d[..., None] * A)
            state = state * dA + (d * u)[..., None] * b[:, None, :]
            y = jnp.einsum('bdn,bn->bd', state, c)
            return (state, y)
        state0 = jnp.zeros((Bsz, d_inner, d_state), x.dtype)
        _, ys = jax.lax.scan(step, state0, (dt_t, B_t, C_t, u_t))
        y = jnp.moveaxis(ys, 0, 2)
        y = y + D[None, :, None] * x
        y = y * silu(z)
        return jnp.swapaxes(y, 1, 2)

    def _L1_ffn_ref(hidden_states, Wr, Wg, Wu, Wd, Sg, Su, Sd, Wsg):
        import jax, jax.numpy as jnp
        import numpy as np
        B, S, H = (2, 256, 512)
        E, K = (8, 2)
        F = 352
        FS = 1408
        NORM_TOPK = False

        def _swiglu(x, wg, wu, wd):
            return jax.nn.silu(x @ wg) * (x @ wu) @ wd
        b, s, h = hidden_states.shape
        x = hidden_states.reshape(-1, h)
        router_logits = x @ Wr
        probs = jax.nn.softmax(router_logits.astype(jnp.float32), axis=-1)
        routing_weights, selected = jax.lax.top_k(probs, K)
        if NORM_TOPK:
            routing_weights = routing_weights / routing_weights.sum(-1, keepdims=True)
        routing_weights = routing_weights.astype(x.dtype)
        C = jnp.einsum('tk,tke->te', routing_weights, jax.nn.one_hot(selected, E, dtype=x.dtype))
        expert_out = jax.vmap(lambda wg, wu, wd: _swiglu(x, wg, wu, wd))(Wg, Wu, Wd)
        moe_out = jnp.einsum('te,eth->th', C, expert_out)
        shared = _swiglu(x, Sg, Su, Sd)
        shared = jax.nn.sigmoid(x @ Wsg) * shared
        out = (moe_out + shared).reshape(b, s, h)
        return out
    x = _layernorm(x + _L0_attn_ref(x, L0_attn_in_proj_w, L0_attn_conv_w, L0_attn_conv_b, L0_attn_x_proj_w, L0_attn_dt_proj_w, L0_attn_dt_proj_b, L0_attn_A_log, L0_attn_D, L0_attn_out_proj_w), axis=-1)
    x = _layernorm(x + _L0_xattn_ref(x, fside_BxS2xS2_0, ctx_1024), axis=-1)
    x = _layernorm(x + _L0_ffn_ref(x, L0_ffn_w_gate, L0_ffn_w_up, L0_ffn_w_down), axis=-1)
    x = _layernorm(x + _L1_attn_ref(x, L1_attn_mu_x, L1_attn_Wx1, L1_attn_Wx2, L1_attn_Wr, L1_attn_Ww1, L1_attn_Ww2, L1_attn_bw, L1_attn_Wk, L1_attn_Wv, L1_attn_Wg, L1_attn_bonus, L1_attn_gn_w, L1_attn_gn_b, L1_attn_Wo), axis=-1)
    x = _layernorm(x + _L1_xattn_ref(ctx_1024, x, L1_xattn_in_proj_w, L1_xattn_conv_w, L1_xattn_conv_b, L1_xattn_x_proj_w, L1_xattn_dt_proj_w, L1_xattn_dt_proj_b, L1_xattn_A_log, L1_xattn_D), axis=-1)
    x = _layernorm(x + _L1_ffn_ref(x, L1_ffn_Wr, L1_ffn_Wg, L1_ffn_Wu, L1_ffn_Wd, L1_ffn_Sg, L1_ffn_Su, L1_ffn_Sd, L1_ffn_Wsg), axis=-1)
    return x

_drawn_inputs = setup_inputs


def setup_inputs(seed=0):
    import zlib

    import numpy as np

    out = dict(_drawn_inputs(seed))
    spreads = {'L0_attn_D': (1.0, 0.6),
     'L1_attn_bw': (0.0, 0.8),
     'L1_attn_gn_w': (1.0, 0.6),
     'L1_attn_gn_b': (0.0, 0.8),
     'L1_xattn_D': (1.0, 0.6)}
    factors = {'L0_attn_conv_b': 4.727,
     'L0_attn_x_proj_w': 7.925,
     'L0_attn_dt_proj_w': 8.0,
     'L0_attn_dt_proj_b': 8.0,
     'L0_attn_A_log': 8.0,
     'L1_attn_mu_x': 6.172,
     'L1_attn_Wx1': 3.328,
     'L1_attn_Wx2': 3.325,
     'L1_attn_Ww1': 8.0,
     'L1_attn_Ww2': 8.0,
     'L1_attn_bonus': 8.0,
     'L1_xattn_in_proj_w': 8.0,
     'L1_xattn_conv_w': 8.0,
     'L1_xattn_conv_b': 8.0,
     'L1_xattn_x_proj_w': 8.0,
     'L1_xattn_dt_proj_w': 8.0,
     'L1_xattn_dt_proj_b': 8.0,
     'L1_xattn_A_log': 8.0,
     'L1_ffn_Wr': 5.544,
     'L1_ffn_Wg': 4.953,
     'L1_ffn_Wu': 4.844,
     'L1_ffn_Wd': 4.838,
     'L1_ffn_Wsg': 6.668}
    for name, (base, spread) in spreads.items():
        noise = np.random.default_rng([zlib.crc32(name.encode()), seed]).standard_normal(out[name].shape)
        drawn = base * np.exp(spread * noise) if base else spread * noise
        out[name] = jnp.asarray(drawn.astype(out[name].dtype))
    for name, factor in factors.items():
        out[name] = (out[name] * factor).astype(out[name].dtype)
    return out
```

```python
from contextlib import ExitStack, contextmanager

import concourse.bass as bass
from concourse import mybir

F32 = mybir.dt.float32
BF16 = mybir.dt.bfloat16
ALU = mybir.AluOpType
ACT = mybir.ActivationFunctionType
AX = mybir.AxisListType

P = 128
T = 512
KM = 4
B = 4
NST = 16
GRP = 4
SLOT = 1536
RING = 3
EPS_LN = 1e-5
EPS_Q = 1e-6
QMAX = 127.0
ROUND = 12582912.0

J0, KI0, TR0 = 8, 4, 128
J1, KI1, TR1 = 4, 2, 16
FFN_TILES = 16
NEXP, FEXP = 8, 352
MOE_TILES = 33
ROUTED = NEXP * FEXP // P

W_OUT0 = 0
W_PREP1 = W_OUT0 + 3
W_FFN = W_PREP1 + 2
W_MIX = W_FFN + FFN_TILES
W_WO = W_MIX + 8
W_PREP0 = W_WO + 2
W_MOE = W_PREP0 + 8
NSLOTS = W_MOE + MOE_TILES

PARAMS = {}
_at = 0
for _name, _n in (("cw0", 4 * J0), ("cb0", J0), ("dtb0", J0), ("d0", J0), ("alog0", NST * J0),
                  ("cw1", 4 * J1), ("cb1", J1), ("dtb1", J1), ("d1", J1), ("alog1", NST * J1),
                  ("mu", KM), ("bw", 2), ("bonus", 2), ("gnw", KM), ("gnb", KM),
                  ("wr", KM * 9), ("rank", NEXP)):
    PARAMS[_name] = (_at, _n)
    _at += _n
NPARAM = _at


def expert_pieces(tile):
    cuts, pieces = {0, P}, []
    for p in range(0, P, 32):
        if (tile * P + p) % FEXP == 0:
            cuts.add(p)
    cuts = sorted(cuts)
    for a, b in zip(cuts, cuts[1:]):
        e = (tile * P + a) // FEXP
        if a == 32:
            pieces += [(32, 64, e), (64, b, e)]
        else:
            pieces.append((a, b, e))
    return pieces


class WeightStream:

    def __init__(self, source, ring, landed, used):
        self.source, self.ring, self.landed, self.used = source, ring, landed, used
        self.first = 0
        self.issued = 0
        self.owed = 0

    def restart(self, first):
        self.first, self.issued, self.owed = first, 0, 0

    def load_until(self, sp, slot, last=NSLOTS):
        while self.first + self.issued < min(slot, last):
            n = self.issued
            if n >= RING:
                sp.wait_ge(self.used, n - RING + 1)
            sp.dma_start(self.ring[:, n % RING, :], self.source[self.first + n]).then_inc(self.landed[n % RING], 16)
            self.issued += 1

    def wait(self, pe, slot):
        n = slot - self.first
        pe.wait_ge(self.landed[n % RING], 16 * (n // RING + 1))
        return self.ring[:, n % RING, :]

    def done(self, slots=1):
        self.owed += slots

    def tell(self, product):
        if self.owed:
            product.then_inc(self.used, self.owed)
            self.owed = 0


class Core:
    pass


def stream_block(k, sp, slots_end, last=NSLOTS):
    k.w.load_until(sp, slots_end + RING - 1, last)


def prepare_scan(nc, k, which, slot, last):
    J, KI, TR = ((J0, KI0, TR0), (J1, KI1, TR1))[which]
    xin = (k.xn, k.ctxT)[which]
    y, dt, dtx = (k.y0, k.dt0, k.dtx0) if which == 0 else (k.y1, k.dt1, k.dtx1)
    gated = which == 0
    NG = J if gated else 0
    tiles_per_slot = 3 if which == 0 else J
    cw, cb, dtb, dd = ((k.cw0, k.cb0, k.dtb0, k.d0), (k.cw1, k.cb1, k.dtb1, k.d1))[which]
    with ExitStack() as ctx:
        def sem(name):
            return k.sem(f"prep{which}_{name}")
        x_in, padded, proj, copied, conv, th, xs = [sem(n) for n in ("x_in", "padded", "proj", "copied", "conv", "th", "xs")]
        gth, gdone, xproj, low, dtp, zread = [sem(n) for n in ("gth", "gdone", "xproj", "low", "dtp", "zread")]
        spexp, spln, dtsum, dtxd, yinit = [sem(n) for n in ("spexp", "spln", "dtsum", "dtxd", "yinit")]
        scratch = k.bc[:, :]
        hp = [scratch[:, i * 516:i * 516 + 515] for i in range(2)]
        v = [scratch[:, 1100 + i * T:1100 + (i + 1) * T] for i in range(2)]
        tt = [scratch[:, 2200 + i * T:2200 + (i + 1) * T] for i in range(2)]
        ts = scratch[0:TR, 3300:3300 + T]
        blk = ctx.enter_context(nc.Block())

        @blk.sync
        def _(sp):
            if which == 0:
                sp.dma_start(k.xn[:], k.x_src).then_inc(x_in, 16)
            stream_block(k, sp, slot + (7 if which == 0 else 2), last)

        @blk.tensor
        def _(pe):
            if which == 0:
                pe.wait_ge(x_in, 16)
            for j in range(J + NG):
                s, at = slot + j // tiles_per_slot, (j % tiles_per_slot) * KI * P
                if j % tiles_per_slot == 0:
                    wt = k.w.wait(pe, s)
                if j >= 4:
                    pe.wait_ge(copied, min(j - 3, J))
                    if j - 4 >= J:
                        pe.wait_ge(gdone, j - 3 - J)
                for c in range(KI):
                    mm = pe.matmul(k.ps[:, j % 4, :], wt[:, at + c * P:at + (c + 1) * P], xin[:, c, :],
                                   start=(c == 0), stop=(c == KI - 1))
                    if c == 0:
                        k.w.tell(mm)
                mm.then_inc(proj, 1)
                if (j % tiles_per_slot == tiles_per_slot - 1 or j == J + NG - 1):
                    k.w.done()
            s = slot + (6 if which == 0 else 1)
            wt = k.w.wait(pe, s)
            pe.wait_ge(xs, J)
            if gated:
                pe.wait_ge(gdone, NG)
            width = TR + 2 * NST
            for c in range(J):
                mm = pe.matmul(k.ps[0:TR, 4, :], wt[:, c * width:c * width + TR], y[:, c, :], start=(c == 0), stop=(c == J - 1))
                k.w.tell(mm)
            for c in range(J):
                mm = pe.matmul(k.ps[0:2 * NST, 5, :], wt[:, c * width + TR:(c + 1) * width], y[:, c, :],
                               start=(c == 0), stop=(c == J - 1))
            mm.then_inc(xproj, 1)
            if which == 0:
                k.w.done()
                wt = k.w.wait(pe, slot + 7)
            at = 0 if which == 0 else J * width
            pe.wait_ge(low, 2)
            for j in range(J):
                if j >= 4:
                    pe.wait_ge(zread, j - 3)
                mm = pe.matmul(k.ps[:, j % 4, :], wt[0:TR, at + j * P:at + (j + 1) * P], ts, start=True, stop=True)
                mm.then_inc(dtp, 1)
            k.w.done()

        @blk.scalar
        def _(act):
            def silu_tanh(j):
                act.wait_ge(conv, 4 * (j + 1))
                if j >= 2:
                    act.wait_ge(xs, j - 1)
                act.activation(tt[j % 2], v[j % 2], ACT.Tanh).then_inc(th, 1)
            act.wait_ge(padded, 1)
            for j in range(J):
                act.wait_ge(proj, j + 1)
                if j >= 2:
                    act.wait_ge(conv, 4 * (j - 1))
                act.activation(hp[j % 2][:, 3:515], k.ps[:, j % 4, :], ACT.Copy).then_inc(copied, 1)
                if j >= 1:
                    silu_tanh(j - 1)
            silu_tanh(J - 1)
            for j in range(NG):
                act.wait_ge(proj, J + j + 1)
                act.wait_ge(xs, J)
                if j >= 2:
                    act.wait_ge(gdone, j - 1)
                act.activation(tt[j % 2], k.ps[:, (J + j) % 4, :], ACT.Tanh, scale=0.5).then_inc(gth, 1)
            act.wait_ge(xproj, 1)
            act.activation(ts, k.ps[0:TR, 4, :], ACT.Copy).then_inc(low, 1)
            act.activation(k.bcs[:], k.ps[0:2 * NST, 5, :], ACT.Copy).then_inc(low, 1)
            for j in range(J):
                act.wait_ge(dtp, j + 1)
                act.activation(dt[:, j, :], k.ps[:, j % 4, :], ACT.Abs, bias=dtb[:, j:j + 1])
                act.activation(dtx[:, j, :], k.ps[:, j % 4, :], ACT.Relu, bias=dtb[:, j:j + 1]).then_inc(zread, 1)
            act.wait_ge(zread, J)
            act.activation(dt[:], dt[:], ACT.Exp, scale=-1.0).then_inc(spexp, 1)
            act.wait_ge(spexp, 1)
            act.activation(dt[:], dt[:], ACT.Ln, bias=1.0).then_inc(spln, 1)

        @blk.vector
        def _(dve):
            dve.memset(scratch[:, 0:3], 0.0)
            dve.memset(scratch[:, 516:519], 0.0).then_inc(padded, 1)
            for j in range(J):
                dve.wait_ge(copied, j + 1)
                if j >= 2:
                    dve.wait_ge(xs, j - 1)
                dve.tensor_scalar(v[j % 2], hp[j % 2][:, 0:T], cw[:, 4 * j:4 * j + 1], cb[:, j:j + 1], ALU.mult, ALU.add).then_inc(conv, 1)
                for c in range(1, 4):
                    dve.wait_ge(conv, 4 * j + c)
                    dve.scalar_tensor_tensor(out=v[j % 2], in0=hp[j % 2][:, c:c + T], scalar=cw[:, 4 * j + c:4 * j + c + 1],
                                             in1=v[j % 2], op0=ALU.mult, op1=ALU.add).then_inc(conv, 1)
                if j >= 1:
                    dve.wait_ge(th, j)
                    dve.scalar_tensor_tensor(out=y[:, j - 1, :], in0=tt[(j - 1) % 2], scalar=1.0, in1=v[(j - 1) % 2],
                                             op0=ALU.add, op1=ALU.mult).then_inc(xs, 1)
            dve.wait_ge(th, J)
            dve.scalar_tensor_tensor(out=y[:, J - 1, :], in0=tt[(J - 1) % 2], scalar=1.0, in1=v[(J - 1) % 2],
                                     op0=ALU.add, op1=ALU.mult).then_inc(xs, 1)
            for j in range(NG):
                dve.wait_ge(gth, j + 1)
                dve.scalar_tensor_tensor(out=k.gs0[:, j, :], in0=tt[j % 2], scalar=1.0, in1=k.ps[:, (J + j) % 4, :],
                                         op0=ALU.add, op1=ALU.mult).then_inc(gdone, 1)
            dve.wait_ge(spln, 1)
            dve.tensor_tensor(dt[:], dt[:], dtx[:], ALU.add).then_inc(dtsum, 1)
            dve.wait_ge(dtsum, 1)
            dve.tensor_tensor(dtx[:], dt[:], y[:], ALU.mult).then_inc(dtxd, 1)
            dve.wait_ge(dtxd, 1)
            for j in range(J):
                dve.tensor_scalar(y[:, j, :], y[:, j, :], dd[:, j:j + 1], None, ALU.mult).then_inc(yinit, 1)


def hidden_and_scan(nc, k, tag, tiles, slot, which, gated, last):
    J = None if which is None else (J0, J1)[which]
    if which is not None:
        y, dt, dtx, aneg = (k.y0, k.dt0, k.dtx0, k.a0) if which == 0 else (k.y1, k.dt1, k.dtx1, k.a1)
    groups = 0 if J is None else (NST // GRP) * J
    with ExitStack() as ctx:
        def sem(name):
            return k.sem(f"{tag}_{name}")
        gate_mm, up_mm, th, silu, hid, hidg, down = [sem(n) for n in ("gate_mm", "up_mm", "th", "silu", "hid", "hidg", "down")]
        bc_mm, bc_in, decay, inp, scanned, read, half, state_sum, summed = [
            sem(n) for n in ("bc_mm", "bc_in", "decay", "inp", "scanned", "read", "half", "state_sum", "summed")]
        blk = ctx.enter_context(nc.Block())
        t2, h2 = k.hid_t, k.hid_h
        bc = k.bc[:, :].rearrange("p (b s n t) -> p b s n t", b=2, s=2, n=GRP)
        hid_ready = hidg if gated else hid

        def gate_slot(jt):
            return k.ps[:, 4 + jt % 2, :]

        up_bank = k.ps[:, 6, :]

        @blk.sync
        def _(sp):
            stream_block(k, sp, slot + tiles, last)

        @blk.tensor
        def _(pe):
            def broadcast(i):
                ng, r = divmod(i, 2 * GRP)
                row = (r // GRP) * NST + ng * GRP + r % GRP
                if i >= 1:
                    pe.wait_ge(bc_in, i)
                pe.matmul(k.ps[:, 7, :], k.ident[0:2 * NST, row:row + 1].broadcast_to([2 * NST, P]), k.bcs[:],
                          start=True, stop=True).then_inc(bc_mm, 1)

            def gate(jt):
                wt = k.w.wait(pe, slot + jt)
                if jt >= 2:
                    pe.wait_ge(silu, jt - 1)
                for c in range(KM):
                    mm = pe.matmul(gate_slot(jt), wt[:, c * P:(c + 1) * P], k.xr[:, c, :], start=(c == 0), stop=(c == KM - 1))
                mm.then_inc(gate_mm, 1)

            def up(jt):
                wt = k.w.wait(pe, slot + jt)
                if jt >= 1:
                    pe.wait_ge(hid, jt)
                for c in range(KM, 2 * KM):
                    mm = pe.matmul(up_bank, wt[:, c * P:(c + 1) * P], k.xr[:, c - KM, :], start=(c == KM), stop=(c == 2 * KM - 1))
                    if c == KM:
                        k.w.tell(mm)
                mm.then_inc(up_mm, 1)

            def down_proj(jt):
                wt = k.w.wait(pe, slot + jt)
                pe.wait_ge(hid_ready, jt + 1)
                for m in range(KM):
                    at = (2 * KM + m) * P
                    mm = pe.matmul(k.ps[:, m, :], wt[:, at:at + P], h2[jt % 2], start=(jt == 0), stop=(jt == tiles - 1))
                    if m == 0:
                        k.w.tell(mm)
                mm.then_inc(down, 1)
                k.w.done()

            todo = [] if J is None else list(range(2 * NST))
            for _ in range(min(len(todo), 2 * GRP)):
                broadcast(todo.pop(0))
            if tiles:
                gate(0)
                up(0)
            per = max(1, -(-2 * GRP // J)) if J else 0
            for step in range(max(tiles, groups)):
                if step + 1 < tiles:
                    gate(step + 1)
                if step < tiles and step >= 1:
                    down_proj(step - 1)
                if step + 1 < tiles:
                    up(step + 1)
                for _ in range(per):
                    if todo and todo[0] < 2 * GRP * (2 + (step // J)):
                        broadcast(todo.pop(0))
            if tiles:
                down_proj(tiles - 1)

        @blk.scalar
        def _(act):
            def copy_row(i):
                ng, r = divmod(i, 2 * GRP)
                act.wait_ge(bc_mm, i + 1)
                if ng >= 2 and r == 0:
                    act.wait_ge(summed, (ng - 1) * J)
                act.activation(bc[:, ng % 2, r // GRP, r % GRP, :], k.ps[:, 7, :], ACT.Copy).then_inc(bc_in, 1)

            def decays(s):
                j, ng = s % J, s // J
                if s >= 2:
                    act.wait_ge(scanned, s - 1)
                for i in range(GRP):
                    n = j * NST + ng * GRP + i
                    a = act.activation(k.da[s % 2][:, i, 1:T], dt[:, j, 1:T], ACT.Exp, scale=aneg[:, n:n + 1])
                a.then_inc(decay, 1)

            rows = [] if J is None else list(range(2 * NST))
            for _ in range(min(len(rows), 2 * GRP)):
                copy_row(rows.pop(0))
            if groups:
                decays(0)
            per = max(1, -(-2 * GRP // J)) if J else 0
            for step in range(max(tiles, groups)):
                if step < tiles:
                    act.wait_ge(gate_mm, step + 1)
                    if step >= 2:
                        act.wait_ge(silu, step - 1)
                    act.activation(t2[step % 2], gate_slot(step), ACT.Tanh, scale=0.5).then_inc(th, 1)
                if step + 1 < groups:
                    decays(step + 1)
                for _ in range(per):
                    if rows and rows[0] < 2 * GRP * (2 + (step // J)):
                        copy_row(rows.pop(0))

        @blk.vector
        def _(dve):
            for step in range(max(tiles, groups)):
                if step < tiles:
                    dve.wait_ge(th, step + 1)
                    dve.scalar_tensor_tensor(out=t2[step % 2], in0=t2[step % 2], scalar=1.0, in1=gate_slot(step),
                                             op0=ALU.add, op1=ALU.mult).then_inc(silu, 1)
                    dve.wait_ge(silu, step + 1)
                    dve.wait_ge(up_mm, step + 1)
                    if step >= 2:
                        dve.wait_ge(down, step - 1)
                    dve.scalar_tensor_tensor(out=h2[step % 2], in0=t2[step % 2], scalar=0.5, in1=up_bank,
                                             op0=ALU.mult, op1=ALU.mult).then_inc(hid, 1)
                    if gated:
                        dve.wait_ge(hid, step + 1)
                        pieces = expert_pieces(step) if step < ROUTED else [(0, P, NEXP)]
                        for a, b, e in pieces:
                            last_op = dve.tensor_tensor(h2[step % 2][a:b, :], h2[step % 2][a:b, :], k.gates[a:b, e, :], ALU.mult)
                        last_op.then_inc(hidg, 1)
                if step < groups:
                    ng = step // J
                    hh = k.hh[step % 2][:, 0:GRP * T]
                    h4 = hh.rearrange("p (n t) -> p n t", n=GRP)
                    dve.wait_ge(decay, step + 1)
                    dve.wait_ge(inp, step + 1)
                    dve.tensor_tensor_scan(hh, k.da[step % 2][:, :, :].rearrange("p n t -> p (n t)"), hh, 0.0,
                                           ALU.mult, ALU.add).then_inc(scanned, 1)
                    dve.wait_ge(scanned, step + 1)
                    dve.wait_ge(bc_in, 2 * GRP * (ng + 1))
                    dve.tensor_tensor(h4, h4, bc[:, ng % 2, 1, :, :], ALU.mult).then_inc(read, 1)
                    dve.wait_ge(read, step + 1)
                    dve.tensor_tensor(h4[:, 0:2, :], h4[:, 0:2, :], h4[:, 2:4, :], ALU.add).then_inc(half, 1)
                    dve.wait_ge(half, step + 1)
                    dve.tensor_tensor(h4[:, 0, :], h4[:, 0, :], h4[:, 1, :], ALU.add).then_inc(state_sum, 1)

        if groups:
            @blk.gpsimd
            def _(pool):
                def inputs(s):
                    j, ng = s % J, s // J
                    h4 = k.hh[s % 2][:, 0:GRP * T].rearrange("p (n t) -> p n t", n=GRP)
                    pool.wait_ge(bc_in, 2 * GRP * ng + GRP)
                    if s >= 2:
                        pool.wait_ge(summed, s - 1)
                    pool.tensor_tensor(h4, bc[:, ng % 2, 0, :, :], dtx[:, j, None, :].broadcast_to([P, GRP, T]), ALU.mult).then_inc(inp, 1)

                inputs(0)
                for s in range(groups):
                    if s + 1 < groups:
                        inputs(s + 1)
                    pool.wait_ge(state_sum, s + 1)
                    if s >= 1:
                        pool.wait_ge(summed, s)
                    pool.tensor_tensor(y[:, s % J, :], y[:, s % J, :], k.hh[s % 2][:, 0:T], ALU.add).then_inc(summed, 1)


def layer_norm(nc, k, tag, parts, slots_end, last, store=None):
    with ExitStack() as ctx:
        def sem(name):
            return k.sem(f"{tag}_{name}")
        res, mean, cent, sq, var, ln, rs, out, stored = [sem(n) for n in ("res", "mean", "cent", "sq", "var", "ln", "rs", "out", "stored")]
        blk = ctx.enter_context(nc.Block())

        @blk.sync
        def _(sp):
            stream_block(k, sp, slots_end, last)
            if store is not None:
                sp.wait_ge(out, KM)
                sp.dma_start(store, k.xr[:]).then_inc(stored, 16)
                sp.wait_ge(stored, 16)

        @blk.tensor
        def _(pe):
            for c in range(KM):
                pe.wait_ge(res, c + 1)
                mm = pe.matmul(k.ps[:, 4, :] if not k.parts_high else k.ps[:, 0, :], k.meanmat[:], k.xc[:, c, :],
                               start=(c == 0), stop=(c == KM - 1))
                if c == 0:
                    k.w.tell(mm)
            mm.then_inc(mean, 1)
            for c in range(KM):
                pe.wait_ge(sq, c + 1)
                mm = pe.matmul(k.ps[:, 5, :] if not k.parts_high else k.ps[:, 1, :], k.meanmat[:], k.xr[:, c, :],
                               start=(c == 0), stop=(c == KM - 1))
            mm.then_inc(var, 1)

        mean_bank = k.ps[:, 0 if k.parts_high else 4, :]
        var_bank = k.ps[:, 1 if k.parts_high else 5, :]

        @blk.scalar
        def _(act):
            for c in range(KM):
                act.wait_ge(cent, c + 1)
                act.activation(k.xr[:, c, :], k.xc[:, c, :], ACT.Square).then_inc(sq, 1)
            act.wait_ge(var, 1)
            act.activation(k.row[:], var_bank, ACT.Ln, bias=k.eps[:, 0:1]).then_inc(ln, 1)
            act.wait_ge(ln, 1)
            act.activation(k.row[:], k.row[:], ACT.Exp, scale=-0.5).then_inc(rs, 1)

        @blk.vector
        def _(dve):
            for c in range(KM):
                dve.tensor_tensor(k.xc[:, c, :], parts[c], k.xr[:, c, :], ALU.add).then_inc(res, 1)
            dve.wait_ge(mean, 1)
            for c in range(KM):
                dve.tensor_tensor(k.xc[:, c, :], k.xc[:, c, :], mean_bank, ALU.subtract).then_inc(cent, 1)
            dve.wait_ge(rs, 1)
            for c in range(KM):
                dve.tensor_tensor(k.xr[:, c, :], k.xc[:, c, :], k.row[:], ALU.mult).then_inc(out, 1)


def finish_mixer0(nc, k, slot, last):
    with ExitStack() as ctx:
        ygate, done, res = k.sem("mix0_ygate"), k.sem("mix0_done"), k.sem("mix0_res")
        blk = ctx.enter_context(nc.Block())

        @blk.sync
        def _(sp):
            stream_block(k, sp, slot + 3, last)

        @blk.gpsimd
        def _(pool):
            pool.tensor_copy(k.xr[:], k.xn[:]).then_inc(res, 1)

        @blk.vector
        def _(dve):
            for j in range(J0):
                dve.scalar_tensor_tensor(out=k.y0[:, j, :], in0=k.y0[:, j, :], scalar=0.5, in1=k.gs0[:, j, :],
                                         op0=ALU.mult, op1=ALU.mult).then_inc(ygate, 1)

        @blk.tensor
        def _(pe):
            for j in range(J0):
                pe.wait_ge(ygate, j + 1)
                for m in range(KM):
                    n = j * KM + m
                    if n % 12 == 0:
                        wt = k.w.wait(pe, slot + n // 12)
                    mm = pe.matmul(k.ps[:, m, :], wt[:, (n % 12) * P:(n % 12 + 1) * P], k.y0[:, j, :], start=(j == 0), stop=(j == J0 - 1))
                    k.w.tell(mm)
                    if n % 12 == 11 or n == J0 * KM - 1:
                        k.w.done()


def quant_linear(nc, k, tag, kt, xt, wt, load, hidden, slots_end, last):
    with ExitStack() as ctx:
        def sem(name):
            return k.sem(f"{tag}_{name}")
        w_in, amax, st, sact, smooth, turned, rmax, sc, q, back, copied, mm_done, scale_bc, bc_copied, out, hth, hact = [
            sem(n) for n in ("w_in", "amax", "st", "sact", "smooth", "turned", "rmax", "sc", "q", "back", "copied",
                             "mm_done", "scale_bc", "bc_copied", "out", "hth", "hact")]
        blk = ctx.enter_context(nc.Block())
        R = k.r0
        n = kt * P
        xs = R[:, 0:2048].rearrange("p (k t) -> p k t", t=T)[:, 0:kt, :]
        ws = R[:, 2048:4096].rearrange("p (k t) -> p k t", t=T)[:, 0:kt, :]
        q1 = R[:, 4096:8192].rearrange("p (c f) -> p c f", c=8)[:, :, 0:n]
        qb = R[:, 8192:10240].bitcast(BF16).rearrange("p (c f) -> p c f", c=8)[:, :, 0:n]
        qT = R[:, 10240:12288].bitcast(BF16).rearrange("p (s k t) -> p s k t", s=2, t=T)
        sm = R[:, 12288:12416]
        H = R[:, 12800:14848].rearrange("p (c t) -> p c t", t=T)
        A = k.xc[:, :, :]
        psb = k.ps[:, :, :].bitcast(BF16)

        def col(i, m=None):
            return sm[:, i * 8:i * 8 + (kt if m is None else m)]

        @blk.sync
        def _(sp):
            if load is not None:
                for dst, src in load:
                    sp.dma_start(dst, src).then_inc(w_in, 16)
            stream_block(k, sp, slots_end, last)

        @blk.vector
        def _(dve):
            step = [0]

            def chain(ins):
                step[0] += 1
                ins.then_inc(st, 1)
                dve.wait_ge(st, step[0])

            dve.tensor_reduce(col(0), xt, AX.X, ALU.max, apply_absolute_value=True).then_inc(amax, 1)
            if load is not None:
                dve.wait_ge(w_in, 16 * len(load))
            dve.tensor_reduce(col(1), wt, AX.X, ALU.max, apply_absolute_value=True).then_inc(amax, 1)
            dve.wait_ge(amax, 2)
            chain(dve.tensor_scalar(col(0), col(0), EPS_Q, None, ALU.max))
            chain(dve.tensor_scalar(col(1), col(1), EPS_Q, None, ALU.max))
            chain(dve.reciprocal(col(2), col(1)))
            dve.tensor_tensor(col(3), col(0), col(2), ALU.mult).then_inc(amax, 1)
            dve.wait_ge(sact, 2)
            chain(dve.tensor_scalar(col(4), col(3), EPS_Q, None, ALU.max))
            chain(dve.reciprocal(col(5), col(4)))
            for c in range(kt):
                dve.tensor_scalar(xs[:, c, :], xt[:, c, :], col(5)[:, c:c + 1], None, ALU.mult).then_inc(smooth, 1)
            for c in range(kt):
                dve.tensor_scalar(ws[:, c, :], wt[:, c, :], col(4)[:, c:c + 1], None, ALU.mult).then_inc(smooth, 1)
            for c in range(8):
                dve.wait_ge(turned, c + 1)
                dve.tensor_reduce(col(6, 8)[:, c:c + 1], k.ps[:, c, 0:n], AX.X, ALU.max, apply_absolute_value=True).then_inc(rmax, 1)
            dve.wait_ge(rmax, 8)
            chain(dve.tensor_scalar(col(7, 8), col(6, 8), EPS_Q, 1.0 / QMAX, ALU.max, ALU.mult))
            sc_ins = dve.reciprocal(col(8, 8), col(7, 8))
            sc_ins.then_inc(sc, 1)
            dve.wait_ge(sc, 1)
            for c in range(8):
                dve.tensor_scalar(q1[:, c, :], k.ps[:, c, 0:n], col(8, 8)[:, c:c + 1], QMAX, ALU.mult, ALU.min).then_inc(q, 1)
            dve.wait_ge(q, 8)
            dve.tensor_scalar(q1, q1, -QMAX, ROUND, ALU.max, ALU.add).then_inc(q, 1)
            dve.wait_ge(q, 9)
            dve.tensor_scalar(qb, q1, ROUND, None, ALU.subtract).then_inc(q, 1)
            dve.wait_ge(bc_copied, 1)
            for oc in range(4):
                dve.wait_ge(mm_done, oc + 1)
                dst = H[:, oc, :] if hidden else A[:, oc, :]
                dve.scalar_tensor_tensor(out=dst, in0=k.ps[:, oc, :], scalar=col(7, 8)[:, 4 + oc:5 + oc], in1=k.row[:],
                                         op0=ALU.mult, op1=ALU.mult).then_inc(out, 1)
            if hidden:
                dve.wait_ge(hth, 1)
                dve.scalar_tensor_tensor(out=A[:, 0:2, :], in0=A[:, 0:2, :], scalar=1.0, in1=H[:, 0:2, :],
                                         op0=ALU.add, op1=ALU.mult).then_inc(hact, 1)
                dve.wait_ge(hact, 1)
                dve.scalar_tensor_tensor(out=A[:, 0:2, :], in0=A[:, 0:2, :], scalar=0.5, in1=H[:, 2:4, :],
                                         op0=ALU.mult, op1=ALU.mult).then_inc(hact, 1)

        @blk.scalar
        def _(act):
            act.wait_ge(amax, 3)
            act.activation(col(3), col(3), ACT.Ln).then_inc(sact, 1)
            act.wait_ge(sact, 1)
            act.activation(col(3), col(3), ACT.Exp, scale=0.5).then_inc(sact, 1)
            for s in range(2):
                for c in range(kt):
                    act.wait_ge(back, s * kt + c + 1)
                    act.activation(qT[:, s, c, :], psb[:, 4 * s + c, 0:T], ACT.Copy).then_inc(copied, 1)
            act.wait_ge(scale_bc, 1)
            act.activation(k.row[:], k.ps[:, 7, :], ACT.Copy).then_inc(bc_copied, 1)
            if hidden:
                act.wait_ge(out, 2)
                act.activation(A[:, 0:2, :], H[:, 0:2, :], ACT.Tanh, scale=0.5).then_inc(hth, 1)

        @blk.tensor
        def _(pe):
            for s, src in enumerate((xs, ws)):
                pe.wait_ge(smooth, (s + 1) * kt)
                for c in range(4):
                    for f in range(kt):
                        mm = pe.transpose(k.ps[:, 4 * s + c, f * P:(f + 1) * P], src[:, f, c * P:(c + 1) * P], k.ident[:])
                        if f == 0:
                            k.w.tell(mm)
                    mm.then_inc(turned, 1)
            pe.wait_ge(q, 10)
            for s in range(2):
                for f in range(kt):
                    for c in range(4):
                        mm = pe.transpose(psb[:, 4 * s + f, c * P:(c + 1) * P], qb[:, 4 * s + c, f * P:(f + 1) * P], k.identb[:])
                    mm.then_inc(back, 1)
            pe.wait_ge(copied, 2 * kt)
            for c in range(4):
                mm = pe.matmul(k.ps[:, 7, c * P:(c + 1) * P], col(7, 8)[:, c:c + 1].broadcast_to([P, P]), k.ident[:],
                               start=True, stop=True)
            mm.then_inc(scale_bc, 1)
            for oc in range(4):
                for f in range(kt):
                    mm = pe.matmul(k.ps[:, oc, :], qT[:, 1, f, oc * P:(oc + 1) * P], qT[:, 0, f, :], start=(f == 0), stop=(f == kt - 1))
                mm.then_inc(mm_done, 1)


def mix_inputs(nc, k, slot, last):
    with ExitStack() as ctx:
        dl, mixed, zmm, zdone = [k.sem(f"mixin_{n}") for n in ("delta", "mixed", "zmm", "zdone")]
        blk = ctx.enter_context(nc.Block())

        @blk.sync
        def _(sp):
            stream_block(k, sp, slot + 1, last)

        @blk.vector
        def _(dve):
            dve.tensor_tensor(k.delta[:, :, 1:T], k.xr[:, :, 0:T - 1], k.xr[:, :, 1:T], ALU.subtract)
            dve.tensor_scalar(k.delta[:, :, 0:1], k.xr[:, :, 0:1], -1.0, None, ALU.mult).then_inc(dl, 1)
            dve.wait_ge(dl, 1)
            for c in range(KM):
                dve.scalar_tensor_tensor(out=k.mx[0][:, c, :], in0=k.delta[:, c, :], scalar=k.mu[:, c:c + 1], in1=k.xr[:, c, :],
                                         op0=ALU.mult, op1=ALU.add).then_inc(mixed, 1)

        @blk.tensor
        def _(pe):
            wt = k.w.wait(pe, slot)
            pe.wait_ge(mixed, KM)
            for i in range(5):
                for c in range(KM):
                    at = c * 160 + i * 32
                    mm = pe.matmul(k.ps[0:32, i, :], wt[:, at:at + 32], k.mx[0][:, c, :], start=(c == 0), stop=(c == KM - 1))
                    if c == 0:
                        k.w.tell(mm)
                mm.then_inc(zmm, 1)
            k.w.done()

        @blk.scalar
        def _(act):
            for i in range(5):
                act.wait_ge(zmm, i + 1)
                act.activation(k.z[:, i, :], k.ps[0:32, i, :], ACT.Tanh).then_inc(zdone, 1)


def mix_projections(nc, k, slot, last):
    with ExitStack() as ctx:
        mus, mus_read, mult, added, outp, taken, low, gth, gdone = [
            k.sem(f"mixp_{n}") for n in ("mus", "mus_read", "mult", "added", "outp", "taken", "low", "gth", "gdone")]
        blk = ctx.enter_context(nc.Block())
        FIRST = {0: 0, 1: 2, 2: 5, 3: 7, 4: 11}

        @blk.sync
        def _(sp):
            stream_block(k, sp, slot + 7, last)

        @blk.tensor
        def _(pe):
            def free_bank(n):
                if n >= 4:
                    pe.wait_ge(taken, n - 3)
                return k.ps[:, 4 + n % 4, :]

            s = slot
            wts = {}
            for i in range(5):
                wt = k.w.wait(pe, s)
                wts[i] = (wt, s)
                for f in range(KM):
                    if i >= 1:
                        pe.wait_ge(mult, (i - 1) * KM + f + 1)
                    pe.matmul(k.ps[:, f, :], wt[0:32, f * P:(f + 1) * P], k.z[:, i, :], start=True, stop=True).then_inc(mus, 1)
                pe.wait_ge(added, KM * (i + 1))
                m = k.mx[i % 2]
                if i == 1:
                    bank = free_bank(2)
                    for c in range(KM):
                        mm = pe.matmul(bank[0:64, :], wt[:, 512 + c * 64:512 + (c + 1) * 64], m[:, c, :], start=(c == 0), stop=(c == KM - 1))
                        if c == 0:
                            k.w.tell(mm)
                    mm.then_inc(outp, 1)
                    pe.wait_ge(low, 1)
                    for o in range(2):
                        mm = pe.matmul(free_bank(3 + o), wt[0:64, 768 + o * P:768 + (o + 1) * P], k.lowrank[:], start=True, stop=True)
                        mm.then_inc(outp, 1)
                    k.w.done()
                    s += 1
                    continue
                outs = 2 if i in (0, 2) else 4
                for o in range(outs):
                    if o == 2:
                        s += 1
                        wt = k.w.wait(pe, s)
                    at = 512 + (o % 2) * KM * P if o < 2 else (o - 2) * KM * P
                    bank = free_bank(FIRST[i] + o)
                    for c in range(KM):
                        mm = pe.matmul(bank, wt[:, at + c * P:at + (c + 1) * P], m[:, c, :], start=(c == 0), stop=(c == KM - 1))
                        if c == 0:
                            k.w.tell(mm)
                    mm.then_inc(outp, 1)
                    if o % 2 == 1:
                        k.w.done()
                s += 1

        @blk.vector
        def _(dve):
            def gates():
                for o in range(4):
                    dve.wait_ge(gth, o + 1)
                    dve.scalar_tensor_tensor(out=k.gg[:, o, :], in0=k.gg[:, o, :], scalar=1.0, in1=k.ps[:, 4 + (11 + o) % 4, :],
                                             op0=ALU.add, op1=ALU.mult).then_inc(gdone, 1)
            for i in range(5):
                for f in range(KM):
                    dve.wait_ge(mus, i * KM + f + 1)
                    if i >= 2 and f == 0:
                        dve.wait_ge(outp, (2, 5, 7, 11)[i - 2])
                    dve.tensor_tensor(k.mx[i % 2][:, f, :], k.delta[:, f, :], k.ps[:, f, :], ALU.mult).then_inc(mult, 1)
            gates()

        @blk.gpsimd
        def _(pool):
            for i in range(5):
                for f in range(KM):
                    pool.wait_ge(mult, i * KM + f + 1)
                    pool.tensor_tensor(k.mx[i % 2][:, f, :], k.mx[i % 2][:, f, :], k.xr[:, f, :], ALU.add).then_inc(added, 1)

        @blk.scalar
        def _(act):
            dst = [k.rr[:, 0, :], k.rr[:, 1, :], None, k.ew[:, 0, :], k.ew[:, 1, :], k.kk[:, 0, :], k.kk[:, 1, :]]
            dst += [k.vv[:, o, :] for o in range(4)]
            for n in range(15):
                act.wait_ge(outp, n + 1)
                bank = k.ps[:, 4 + n % 4, :]
                if n == 2:
                    act.activation(k.lowrank[:], bank[0:64, :], ACT.Tanh).then_inc(low, 1)
                    act.wait_ge(low, 1)
                    act.activation(k.junk[:, 0:1], k.eps[:, 0:1], ACT.Copy).then_inc(taken, 1)
                elif n in (3, 4):
                    act.activation(dst[n], bank, ACT.Exp, bias=k.bw[:, n - 3:n - 2]).then_inc(taken, 1)
                elif n < 11:
                    act.activation(dst[n], bank, ACT.Copy).then_inc(taken, 1)
                else:
                    act.activation(k.gg[:, n - 11, :], bank, ACT.Tanh, scale=0.5).then_inc(gth, 1)


def mix_scan(nc, k, slots_end, last):
    with ExitStack() as ctx:
        rb, rz, decay, vb, kv, scanned, prod, red, zero = [
            k.sem(f"mixs_{n}") for n in ("rb", "rz", "decay", "vb", "kv", "scanned", "prod", "red", "zero")]
        blk = ctx.enter_context(nc.Block())
        G = 8
        kvb = [k.bc[:, i * 2048:(i + 1) * 2048] for i in range(2)]

        @blk.sync
        def _(sp):
            stream_block(k, sp, slots_end, last)

        @blk.scalar
        def _(act):
            for q in range(2):
                for i in range(4):
                    a = act.activation(k.da[q][:, i, 1:T], k.ew[:, q, 1:T], ACT.Exp, scale=-1.0)
                a.then_inc(decay, 1)

        @blk.gpsimd
        def _(pool):
            pool.memset(k.hh[0][:, 0:1], 0.0)
            pool.memset(k.hh[1][:, 0:1], 0.0).then_inc(zero, 1)
            pool.wait_ge(zero, 1)
            pool.wait_ge(rz, 1)
            for g in range(G):
                q = g // 4
                pool.wait_ge(scanned, g + 1)
                pool.tensor_tensor(kvb[g % 2].rearrange("p (v t) -> p v t", v=4),
                                   k.hh[g % 2][:, 0:2048].rearrange("p (v t) -> p v t", v=4),
                                   k.rr[:, q, None, :].broadcast_to([P, 4, T]), ALU.mult).then_inc(prod, 1)

        @blk.vector
        def _(dve):
            for q in range(2):
                dve.scalar_tensor_tensor(out=k.rbk[:, q, :], in0=k.rr[:, q, :], scalar=k.bonus[:, q:q + 1], in1=k.kk[:, q, :],
                                         op0=ALU.mult, op1=ALU.mult).then_inc(rb, 1)
            dve.wait_ge(rb, 2)
            dve.memset(k.rr[:, :, 0:1], 0.0).then_inc(rz, 1)
            dve.wait_ge(zero, 1)
            for g in range(G):
                q = g // 4
                dve.wait_ge(vb, g + 1)
                if g >= 2:
                    dve.wait_ge(red, g - 1)
                dve.tensor_tensor(kvb[g % 2].rearrange("p (v t) -> p v t", v=4), k.ps[:, 4:8, :],
                                  k.kk[:, q, None, :].broadcast_to([P, 4, T]), ALU.mult).then_inc(kv, 1)
                dve.wait_ge(kv, g + 1)
                dve.wait_ge(decay, q + 1)
                if g >= 2:
                    dve.wait_ge(prod, g - 1)
                dve.tensor_tensor_scan(k.hh[g % 2][:, 1:2049], k.da[q][:, :, :].rearrange("p v t -> p (v t)"), kvb[g % 2], 0.0,
                                       ALU.mult, ALU.add).then_inc(scanned, 1)

        @blk.tensor
        def _(pe):
            def spread(g):
                q, m = divmod(g, 4)
                if g >= 1:
                    pe.wait_ge(kv, g)
                for i in range(4):
                    sel = k.key_rows[q][32 * i:32 * i + 32, :]
                    mm = pe.matmul(k.ps[:, 4 + i, :], sel, k.vv[32 * i:32 * i + 32, m, :], start=True, stop=True)
                    if i == 0:
                        k.w.tell(mm)
                mm.then_inc(vb, 1)

            spread(0)
            for g in range(G):
                q, m = divmod(g, 4)
                if g + 1 < G:
                    spread(g + 1)
                pe.wait_ge(prod, g + 1)
                for i in range(4):
                    mm = pe.matmul(k.ps[32 * i:32 * i + 32, m, :], k.key_sum[q][:, 0:32], kvb[g % 2][:, i * T:(i + 1) * T],
                                   start=(q == 0), stop=(q == 1), skip_group_check=True)
                mm.then_inc(red, 1)


def mix_output(nc, k, slot, last):
    with ExitStack() as ctx:
        bon, bv, osum, mean, cent, sq, var, ln, rs, nrm, aff, gat = [
            k.sem(f"mixo_{n}") for n in ("bon", "bv", "osum", "mean", "cent", "sq", "var", "ln", "rs", "nrm", "aff", "gat")]
        blk = ctx.enter_context(nc.Block())
        o = k.oo

        @blk.sync
        def _(sp):
            stream_block(k, sp, slot + 2, last)

        @blk.tensor
        def _(pe):
            for q in range(2):
                mm = pe.matmul(k.ps[:, 4, :], k.key_sum[q], k.rbk[:, q, :], start=(q == 0), stop=(q == 1))
            mm.then_inc(bon, 1)
            pe.wait_ge(osum, KM)
            for c in range(KM):
                mm = pe.matmul(k.ps[:, 5, :], k.headmean[:], o[:, c, :], start=(c == 0), stop=(c == KM - 1))
            mm.then_inc(mean, 1)
            for c in range(KM):
                pe.wait_ge(sq, c + 1)
                mm = pe.matmul(k.ps[:, 6, :], k.headmean[:], k.xc[:, c, :], start=(c == 0), stop=(c == KM - 1))
            mm.then_inc(var, 1)
            for c in range(KM):
                if c % 2 == 0:
                    wt = k.w.wait(pe, slot + c // 2)
                pe.wait_ge(gat, c + 1)
                for m in range(KM):
                    at = ((c % 2) * KM + m) * P
                    mm = pe.matmul(k.ps[:, m, :], wt[:, at:at + P], o[:, c, :], start=(c == 0), stop=(c == KM - 1))
                    k.w.tell(mm)
                if c % 2 == 1:
                    k.w.done()

        @blk.vector
        def _(dve):
            dve.wait_ge(bon, 1)
            for c in range(KM):
                dve.tensor_tensor(o[:, c, :], k.vv[:, c, :], k.ps[:, 4, :], ALU.mult).then_inc(bv, 1)
            for c in range(KM):
                dve.wait_ge(bv, c + 1)
                dve.tensor_tensor(o[:, c, :], o[:, c, :], k.ps[:, c, :], ALU.add).then_inc(osum, 1)
            dve.wait_ge(mean, 1)
            for c in range(KM):
                dve.tensor_tensor(o[:, c, :], o[:, c, :], k.ps[:, 5, :], ALU.subtract).then_inc(cent, 1)
            dve.wait_ge(rs, 1)
            for c in range(KM):
                dve.tensor_tensor(o[:, c, :], o[:, c, :], k.row[:], ALU.mult).then_inc(nrm, 1)
            for c in range(KM):
                dve.wait_ge(nrm, c + 1)
                dve.tensor_scalar(o[:, c, :], o[:, c, :], k.gnw[:, c:c + 1], k.gnb[:, c:c + 1], ALU.mult, ALU.add).then_inc(aff, 1)
            for c in range(KM):
                dve.wait_ge(aff, c + 1)
                dve.scalar_tensor_tensor(out=o[:, c, :], in0=o[:, c, :], scalar=0.5, in1=k.gg[:, c, :],
                                         op0=ALU.mult, op1=ALU.mult).then_inc(gat, 1)

        @blk.scalar
        def _(act):
            for c in range(KM):
                act.wait_ge(cent, c + 1)
                act.activation(k.xc[:, c, :], o[:, c, :], ACT.Square).then_inc(sq, 1)
            act.wait_ge(var, 1)
            act.activation(k.row[:], k.ps[:, 6, :], ACT.Ln, bias=k.eps[:, 0:1]).then_inc(ln, 1)
            act.wait_ge(ln, 1)
            act.activation(k.row[:], k.row[:], ACT.Exp, scale=-0.5).then_inc(rs, 1)


def finish_mixer1(nc, k, slots_end, last):
    with ExitStack() as ctx:
        turned, th, zg, yz = [k.sem(f"x1_{n}") for n in ("turned", "th", "zg", "yz")]
        blk = ctx.enter_context(nc.Block())

        @blk.sync
        def _(sp):
            stream_block(k, sp, slots_end, last)

        @blk.tensor
        def _(pe):
            for c in range(4):
                for f in range(KM):
                    mm = pe.transpose(k.ps[:, c, f * P:(f + 1) * P], k.xr[:, f, c * P:(c + 1) * P], k.ident[:])
                mm.then_inc(turned, 1)

        @blk.scalar
        def _(act):
            for c in range(4):
                act.wait_ge(turned, c + 1)
                act.activation(k.xc[:, c, :], k.ps[:, c, :], ACT.Tanh, scale=0.5).then_inc(th, 1)

        @blk.vector
        def _(dve):
            for c in range(4):
                dve.wait_ge(th, c + 1)
                dve.scalar_tensor_tensor(out=k.xc[:, c, :], in0=k.xc[:, c, :], scalar=1.0, in1=k.ps[:, c, :],
                                         op0=ALU.add, op1=ALU.mult).then_inc(zg, 1)
                dve.wait_ge(zg, c + 1)
                dve.scalar_tensor_tensor(out=k.y1[:, c, :], in0=k.xc[:, c, :], scalar=0.5, in1=k.y1[:, c, :],
                                         op0=ALU.mult, op1=ALU.mult).then_inc(yz, 1)


def route(nc, k, slots_end, last):
    with ExitStack() as ctx:
        logits, st, ex, exd, sg, sgd, gates, gmm, gcopy = [
            k.sem(f"route_{n}") for n in ("logits", "st", "ex", "exd", "sg", "sgd", "gates", "gmm", "gcopy")]
        blk = ctx.enter_context(nc.Block())
        S = k.xc[:, 0, :]

        def buf(i, w=NEXP):
            return S[:, i * 40:i * 40 + 4 * w].rearrange("p (c e) -> p c e", c=4)

        @blk.sync
        def _(sp):
            stream_block(k, sp, slots_end, last)

        @blk.tensor
        def _(pe):
            for c in range(4):
                for f in range(KM):
                    mm = pe.matmul(k.ps[:, 0, c * 16:c * 16 + 9], k.xr[:, f, c * P:(c + 1) * P], k.wr[:, f * 9:(f + 1) * 9],
                                   start=(f == 0), stop=(f == KM - 1))
                    if f == 0:
                        k.w.tell(mm)
            mm.then_inc(logits, 1)
            pe.wait_ge(gates, 1)
            for e in range(NEXP + 1):
                if e >= 4:
                    pe.wait_ge(gcopy, e - 3)
                for c in range(4):
                    mm = pe.matmul(k.ps[:, 1 + e % 4, c * P:(c + 1) * P], buf(9, 9)[:, c, e:e + 1].broadcast_to([P, P]), k.ident[:],
                                   start=True, stop=True)
                mm.then_inc(gmm, 1)

        @blk.vector
        def _(dve):
            step = [0]

            def chain(ins):
                step[0] += 1
                ins.then_inc(st, 1)
                dve.wait_ge(st, step[0])

            def over(col):
                return col.broadcast_to([P, 4, NEXP])

            lg = k.ps[:, 0, 0:64].rearrange("p (c e) -> p c e", c=4)
            mx, key_max = buf(1, 1), buf(2, 1)
            dve.wait_ge(logits, 1)
            chain(dve.tensor_reduce(mx, lg[:, :, 0:NEXP], AX.X, ALU.max))
            dve.tensor_tensor(buf(0), lg[:, :, 0:NEXP], over(mx), ALU.subtract).then_inc(ex, 1)
            dve.wait_ge(exd, 1)
            chain(dve.tensor_reduce(mx, buf(0), AX.X, ALU.add))
            chain(dve.reciprocal(key_max, mx))
            chain(dve.tensor_tensor(buf(3), buf(0), over(key_max), ALU.mult))
            rank = k.rank[:, None, :].broadcast_to([P, 4, NEXP])
            chain(dve.tensor_copy(buf(4), buf(3)))
            for i in range(2):
                chain(dve.tensor_reduce(mx, buf(4), AX.X, ALU.max))
                chain(dve.tensor_tensor(buf(5), buf(4), over(mx), ALU.is_equal))
                chain(dve.tensor_tensor(buf(5), buf(5), rank, ALU.mult))
                chain(dve.tensor_reduce(key_max, buf(5), AX.X, ALU.max))
                chain(dve.tensor_tensor(buf(6 + i), buf(5), over(key_max), ALU.is_equal))
                if i == 0:
                    chain(dve.scalar_tensor_tensor(out=buf(4), in0=buf(6), scalar=-2.0, in1=buf(4), op0=ALU.mult, op1=ALU.add))
            chain(dve.tensor_tensor(buf(6), buf(6), buf(7), ALU.add))
            chain(dve.tensor_tensor(buf(9, 9)[:, :, 0:NEXP], buf(6), buf(3), ALU.mult))
            dve.wait_ge(sgd, 1)
            dve.tensor_scalar(buf(9, 9)[:, :, NEXP:NEXP + 1], buf(8, 1), 1.0, 0.5, ALU.add, ALU.mult).then_inc(gates, 1)

        @blk.scalar
        def _(act):
            lg = k.ps[:, 0, 0:64].rearrange("p (c e) -> p c e", c=4)
            act.wait_ge(ex, 1)
            act.activation(buf(8, 1), lg[:, :, NEXP:NEXP + 1], ACT.Tanh, scale=0.5).then_inc(sgd, 1)
            act.activation(buf(0), buf(0), ACT.Exp).then_inc(exd, 1)
            for e in range(NEXP + 1):
                act.wait_ge(gmm, e + 1)
                act.activation(k.gates[:, e, :], k.ps[:, 1 + e % 4, :], ACT.Copy).then_inc(gcopy, 1)


def set_constants(nc, k, params_src, squares_src):
    with ExitStack() as ctx:
        p_in, ready, rate, neg = [k.sem(f"const_{n}") for n in ("p_in", "ready", "rate", "neg")]
        blk = ctx.enter_context(nc.Block())

        @blk.sync
        def _(sp):
            sp.dma_start(k.params[:], params_src).then_inc(p_in, 16)
            sp.dma_start(k.squares[:], squares_src).then_inc(p_in, 16)

        @blk.gpsimd
        def _(pool):
            pool.memset(k.da[0][:, :, 0:1], 0.0)
            pool.memset(k.da[1][:, :, 0:1], 0.0).then_inc(ready, 1)
            pool.memset(k.eps[:], EPS_LN).then_inc(ready, 1)

        @blk.scalar
        def _(act):
            act.wait_ge(p_in, 32)
            act.activation(k.a0, k.a0, ACT.Exp)
            act.activation(k.a1, k.a1, ACT.Exp).then_inc(rate, 1)

        @blk.vector
        def _(dve):
            dve.wait_ge(p_in, 32)
            for taps in (k.cw0, k.cb0, k.cw1, k.cb1):
                dve.tensor_scalar(taps, taps, 0.5, None, ALU.mult)
            dve.tensor_copy(k.identb[:], k.ident[:]).then_inc(neg, 1)
            dve.wait_ge(rate, 1)
            dve.tensor_scalar(k.a0, k.a0, -1.0, None, ALU.mult)
            dve.tensor_scalar(k.a1, k.a1, -1.0, None, ALU.mult).then_inc(neg, 1)


def decoder(nc, xT, guwT, ctxT, wstream, params, squares, out):
    with ExitStack() as ctx:
        k = Core()

        def sb(name, shape, dt=F32):
            h = ctx.enter_context(nc.sbuf_tensor(name, shape, dt))
            return h[:, :, :] if len(shape) == 3 else h[:, :]

        r0 = sb("r0", [P, 16384])
        r1 = sb("r1", [P, 6144])
        k.r0 = r0
        tiles = lambda reg, a, n: reg[:, a:a + n * T].rearrange("p (j t) -> p j t", t=T)
        k.y0, k.gs0, k.dt0, k.dtx0 = [tiles(r0, i * 4096, 8) for i in range(4)]
        k.delta, k.vv, k.gg, k.oo = [tiles(r0, i * 2048, 4) for i in range(4)]
        k.rr, k.kk, k.ew, k.rbk = [tiles(r0, 8192 + i * 1024, 2) for i in range(4)]
        k.lowrank = r0[0:64, 12288:12288 + T]
        k.junk = r0[:, 12800:12801]
        k.y1, k.dt1, k.dtx1 = [tiles(r1, i * 2048, 4) for i in range(3)]
        k.z = r1[0:32, 2048:2048 + 5 * T].rearrange("p (i t) -> p i t", t=T)
        k.gates = tiles(r1, 0, 9)
        k.xn, k.xr, k.xc = [sb(n, [P, KM, T]) for n in ("xn", "xr", "xc")]
        k.ctxT = sb("ctxTs", [P, 2, T])
        k.da = [sb(f"da{i}", [P, GRP, T]) for i in range(2)]
        k.hh = [sb(f"hh{i}", [P, GRP * T + 8]) for i in range(2)]
        k.bc = sb("bc", [P, 8192])
        k.mx = [tiles(k.bc, i * 2048, 4) for i in range(2)]
        k.hid_t = [k.xc[:, i, :] for i in range(2)]
        k.hid_h = [k.xc[:, 2 + i, :] for i in range(2)]
        k.row = sb("row", [P, T])
        k.bcs = sb("bcs", [2 * NST, T])
        k.eps = sb("eps", [P, 1])
        k.params = sb("params_sb", [P, NPARAM])
        k.squares = sb("squares_sb", [P, 7, P])
        k.ident, k.meanmat, k.headmean = [k.squares[:, i, :] for i in range(3)]
        k.key_sum, k.key_rows = [[k.squares[:, 3 + 2 * i + q, :] for q in range(2)] for i in range(2)]
        k.identb = sb("identb", [P, P], BF16)
        def param(name):
            at, n = PARAMS[name]
            return k.params[:, at:at + n]

        k.cw0, k.cb0, k.dtb0, k.d0, k.a0 = [param(n) for n in ("cw0", "cb0", "dtb0", "d0", "alog0")]
        k.cw1, k.cb1, k.dtb1, k.d1, k.a1 = [param(n) for n in ("cw1", "cb1", "dtb1", "d1", "alog1")]
        k.mu, k.bw, k.bonus, k.gnw, k.gnb = [param(n) for n in ("mu", "bw", "bonus", "gnw", "gnb")]
        k.wr, k.rank = param("wr"), param("rank")
        ring = sb("ring", [P, RING, SLOT])
        k.ps = ctx.enter_context(nc.psum_tensor("ps", [P, 8, T], F32))[:, :, :]
        k.parts_high = False

        @contextmanager
        def cleared(weights_from=None):
            with ExitStack() as own:
                held, outer = [], k.sem

                def sem(name):
                    held.append(own.enter_context(nc.semaphore(name)))
                    return held[-1]
                if weights_from is not None:
                    k.w = WeightStream(wstream, ring, [sem(f"w_landed{i}") for i in range(RING)], sem("w_used"))
                    k.w.restart(weights_from)
                k.sem = sem
                yield
                k.sem = outer
                with nc.Block() as blk:
                    @blk.gpsimd
                    def _(pool):
                        for s in held:
                            pool.sem_clear(s)

        k.sem = None
        with cleared(W_PREP0):
            set_constants(nc, k, params, squares)
            k.x_src = xT[0]
            prepare_scan(nc, k, 0, W_PREP0, W_MOE)
            hidden_and_scan(nc, k, "first", 0, W_MOE, 0, False, W_MOE)
        banks = [k.ps[:, c, :] for c in range(KM)]

        with nc.Fori(0, B) as b:
            with cleared(0):
                with cleared():
                    finish_mixer0(nc, k, W_OUT0, NSLOTS)
                    layer_norm(nc, k, "ln0", banks, W_PREP1, NSLOTS)
                    guw = k.bc[:, 0:KM * T].rearrange("p (c t) -> p c t", t=T)
                    quant_linear(nc, k, "q0", KM, k.xr, guw, [(guw, guwT[b]), (k.ctxT, ctxT[b])], True, W_PREP1, NSLOTS)
                    quant_linear(nc, k, "q1", 2, k.xc[:, 0:2, :], k.ctxT, None, False, W_PREP1, NSLOTS)
                    layer_norm(nc, k, "ln1", [k.xc[:, c, :] for c in range(KM)], W_PREP1, NSLOTS)
                with cleared():
                    prepare_scan(nc, k, 1, W_PREP1, NSLOTS)
                    hidden_and_scan(nc, k, "ffn", FFN_TILES, W_FFN, 1, False, NSLOTS)
                    layer_norm(nc, k, "ln2", banks, W_MIX, NSLOTS)
                    mix_inputs(nc, k, W_MIX, NSLOTS)
                    mix_projections(nc, k, W_MIX + 1, NSLOTS)
                with cleared():
                    mix_scan(nc, k, W_WO, NSLOTS)
                    mix_output(nc, k, W_WO, NSLOTS)
                    layer_norm(nc, k, "ln3", banks, W_PREP0, NSLOTS)
                    finish_mixer1(nc, k, W_PREP0, NSLOTS)
                    layer_norm(nc, k, "ln4", [k.y1[:, c, :] for c in range(KM)], W_PREP0, NSLOTS)
                with cleared():
                    k.x_src = xT[b + 1]
                    prepare_scan(nc, k, 0, W_PREP0, NSLOTS)
                    route(nc, k, W_MOE, NSLOTS)
                    hidden_and_scan(nc, k, "moe", MOE_TILES, W_MOE, 0, True, NSLOTS)
                    layer_norm(nc, k, "ln5", banks, NSLOTS, NSLOTS, store=out[b])


def _cols(a, n):
    return a.reshape(n, P, -1).transpose(1, 0, 2).reshape(P, -1)


def _tiles(np, w, kt, ot, out_major=True):
    t = w.reshape(kt, P, ot, P)
    return (t.transpose(1, 2, 0, 3) if out_major else t.transpose(1, 0, 2, 3)).reshape(P, kt * ot * P)


def _slots(np, i):
    def pad(*parts):
        s = np.zeros((P, SLOT), np.float32)
        at = 0
        for p in parts:
            s[:p.shape[0], at:at + p.shape[1]] = p
            at += p.shape[1]
        return s

    def split(w, cols, n):
        return [pad(w[:, j * cols:min((j + 1) * cols, w.shape[1])]) for j in range(n)]

    by_v = lambda w: w.reshape(T, 32, 16).transpose(0, 2, 1).reshape(T, T)
    s = split(_tiles(np, i["L0_attn_out_proj_w"].T, J0, KM, False), SLOT, 3)
    s += [pad(_tiles(np, i["L1_xattn_in_proj_w"].T, 2, 4)),
          pad(_cols(i["L1_xattn_x_proj_w"].T, 4), i["L1_xattn_dt_proj_w"].T)]

    def hidden(g, u, d):
        n = g.shape[1] // P
        return [pad(_tiles(np, g[:, j * P:(j + 1) * P], KM, 1), _tiles(np, u[:, j * P:(j + 1) * P], KM, 1), d[j * P:(j + 1) * P])
                for j in range(n)]

    s += hidden(i["L0_ffn_w_gate"].T, i["L0_ffn_w_up"].T, i["L0_ffn_w_down"].T)
    wx2 = i["L1_attn_Wx2"]
    pad_rows = lambda a: np.concatenate([a, np.zeros((P - a.shape[0], a.shape[1]), a.dtype)])
    s += [pad(_cols(i["L1_attn_Wx1"], KM)),
          pad(pad_rows(wx2[0]), _tiles(np, i["L1_attn_Wr"], KM, 2)),
          pad(pad_rows(wx2[1]), _cols(i["L1_attn_Ww1"], KM), i["L1_attn_Ww2"]),
          pad(pad_rows(wx2[2]), _tiles(np, i["L1_attn_Wk"], KM, 2))]
    for n, name in ((3, "L1_attn_Wv"), (4, "L1_attn_Wg")):
        w = _tiles(np, by_v(i[name]), KM, 4)
        s += [pad(pad_rows(wx2[n]), w[:, 0:1024]), pad(w[:, 1024:2048])]
    wo = i["L1_attn_Wo"].reshape(32, 16, T).transpose(1, 0, 2).reshape(T, T)
    s += split(_tiles(np, wo, KM, 4, False), 1024, 2)
    s += split(_tiles(np, i["L0_attn_in_proj_w"].T, KM, 16), SLOT, 6)
    s += [pad(_cols(i["L0_attn_x_proj_w"].T, J0)), pad(i["L0_attn_dt_proj_w"].T)]
    side = lambda a: a.transpose(1, 0, 2).reshape(T, NEXP * FEXP)
    s += hidden(side(i["L1_ffn_Wg"]), side(i["L1_ffn_Wu"]), i["L1_ffn_Wd"].reshape(NEXP * FEXP, T))
    s += hidden(i["L1_ffn_Sg"], i["L1_ffn_Su"], i["L1_ffn_Sd"])
    return np.stack(s)


def _params(np, i):
    v = {
        "cw0": _cols(i["L0_attn_conv_w"], J0), "cb0": _cols(i["L0_attn_conv_b"], J0), "dtb0": _cols(i["L0_attn_dt_proj_b"], J0),
        "d0": _cols(i["L0_attn_D"], J0), "alog0": _cols(i["L0_attn_A_log"], J0),
        "cw1": _cols(i["L1_xattn_conv_w"].reshape(T, 4), J1), "cb1": _cols(i["L1_xattn_conv_b"], J1),
        "dtb1": _cols(i["L1_xattn_dt_proj_b"], J1), "d1": _cols(i["L1_xattn_D"], J1), "alog1": _cols(i["L1_xattn_A_log"], J1),
        "mu": _cols(i["L1_attn_mu_x"], KM), "bw": _cols(i["L1_attn_bw"], 2),
        "bonus": _cols(i["L1_attn_bonus"].reshape(-1), 2),
        "gnw": np.repeat(i["L1_attn_gn_w"].reshape(KM, 4), 32, axis=1).T, "gnb": np.repeat(i["L1_attn_gn_b"].reshape(KM, 4), 32, axis=1).T,
        "wr": _cols(np.concatenate([i["L1_ffn_Wr"], i["L1_ffn_Wsg"]], axis=1), KM),
        "rank": np.tile(np.arange(NEXP, 0, -1, dtype=np.float32), (P, 1)),
    }
    return np.ascontiguousarray(np.concatenate([v[n].reshape(P, PARAMS[n][1]) for n in PARAMS], axis=1))


def kernel(**inputs):
    import numpy as np
    import concourse.bacc as bacc
    from concourse.bass_utils import run_bass_kernel_spmd as run

    i = {n: np.asarray(a) for n, a in inputs.items()}
    turned = lambda a, kt: np.ascontiguousarray(a.transpose(0, 2, 1).reshape(B, kt, P, T).transpose(0, 2, 1, 3))
    xT = turned(i["x"], KM)
    own = [np.eye(32)[16 * q + np.arange(P) // 8] for q in range(2)]
    squares = np.stack([np.eye(P), np.full((P, P), 1 / T), np.tile(np.eye(32), (4, 4)) / 16, *(np.tile(m, (1, 4)) for m in own),
                        *(np.tile(m.T, (4, 1)) for m in own)], 1).astype(np.float32)
    arrays = {
        "xT": np.concatenate([xT, xT[:1]]),
        "guwT": turned(i["fside_BxS2xS2_0"], KM),
        "ctxT": turned(i["ctx_1024"], 2),
        "wstream": _slots(np, i),
        "params": _params(np, i),
        "squares": squares,
    }
    nc = bacc.Bacc("TRN2", target_bir_lowering=False, num_devices=1)
    args = {n: nc.dram_tensor(n, a.shape, mybir.dt.from_np(a.dtype), kind="ExternalInput").ap() for n, a in arrays.items()}
    out = nc.dram_tensor("out", (B, P, KM, T), F32, kind="ExternalOutput").ap()
    decoder(nc, out=out, **args)
    r = run(nc, [arrays], core_ids=[0])
    o = r.results[0]["out"]
    return np.ascontiguousarray(o.transpose(0, 3, 2, 1).reshape(B, T, T))
```
